# Optimizing a Trainium2 kernel written in Bass

```python
import numpy as np
import jax
import jax.numpy as jnp

def _softmax(x, axis=-1):
    return jax.nn.softmax(x, axis=axis)

def _gelu(x):
    return jax.nn.gelu(x, approximate=True)

def _silu(x):
    return jax.nn.silu(x)

def _sigmoid(x):
    return jax.nn.sigmoid(x)

def _layernorm(x, axis=-1, eps=1e-05):
    m = jnp.mean(x, axis=axis, keepdims=True)
    v = jnp.var(x, axis=axis, keepdims=True)
    return (x - m) / jnp.sqrt(v + eps)

def _scatter_add(tgt, idx, src, axis=0):
    return tgt.at[idx].add(src)

def _segment_sum(src, seg, n):
    return jax.ops.segment_sum(src, seg, n)
kernel_name = 'mk_sandwich_d1_jaxref_r8_a4df50'

def setup_inputs(seed: int=0):
    np.random.seed(seed)
    _w = jnp.asarray

    def _L0_attn_setup():
        import jax, jax.numpy as jnp
        import numpy as np
        N_HEADS = 16
        CHUNK = 128

        def _phi(x):
            return jax.nn.elu(x) + 1.0
        key = jax.random.key(seed)
        ks = jax.random.split(key, 5)
        d = 128
        scale = (2.0 / (d + d)) ** 0.5
        W = lambda k: jax.random.normal(k, (d, d), jnp.float32) * scale
        return {'x': jax.random.normal(ks[0], (4, 512, d), jnp.float32), 'Wq': W(ks[1]), 'bq': jnp.zeros((d,), jnp.float32), 'Wk': W(ks[2]), 'bk': jnp.zeros((d,), jnp.float32), 'Wv': W(ks[3]), 'bv': jnp.zeros((d,), jnp.float32), 'Wo': W(ks[4]), 'bo': jnp.zeros((d,), jnp.float32)}
    _L0_attn_in = _L0_attn_setup()

    def _L0_ffn_setup():
        import jax, jax.numpy as jnp
        import numpy as np
        B, S, H, F, G = (8, 256, 128, 512, 128)
        EPS = 1e-05

        def _dequant(q, scales, g):
            K, N = q.shape
            w = (q.astype(jnp.float32) - 128.0).reshape(K // g, g, N) * scales[:, None, :]
            return w.reshape(K, N)
        key = jax.random.key(seed)
        ks = jax.random.split(key, 8)
        x = jax.random.normal(ks[0], (B, S, H), dtype=jnp.float32)
        ln_gamma = jnp.ones((H,), jnp.float32)
        ln_beta = jnp.zeros((H,), jnp.float32)
        fc1_q = jax.random.randint(ks[1], (H, F), 0, 32, dtype=jnp.int32)
        fc2_q = jax.random.randint(ks[2], (F, H), 0, 32, dtype=jnp.int32)
        fc1_scales = jax.random.uniform(ks[3], (H // G, F), jnp.float32) * 0.02 + 0.001
        fc2_scales = jax.random.uniform(ks[4], (F // G, H), jnp.float32) * 0.02 + 0.001
        fc1_bias = jax.random.normal(ks[5], (F,), jnp.float32) * 0.02
        fc2_bias = jax.random.normal(ks[6], (H,), jnp.float32) * 0.02
        return {'x': x, 'ln_gamma': ln_gamma, 'ln_beta': ln_beta, 'fc1_q': fc1_q, 'fc1_scales': fc1_scales, 'fc1_bias': fc1_bias, 'fc2_q': fc2_q, 'fc2_scales': fc2_scales, 'fc2_bias': fc2_bias}
    _L0_ffn_in = _L0_ffn_setup()
    _d = {'L0_attn_x': _L0_attn_in['x'], 'L0_attn_Wq': _L0_attn_in['Wq'], 'L0_attn_bq': _L0_attn_in['bq'], 'L0_attn_Wk': _L0_attn_in['Wk'], 'L0_attn_bk': _L0_attn_in['bk'], 'L0_attn_Wv': _L0_attn_in['Wv'], 'L0_attn_bv': _L0_attn_in['bv'], 'L0_attn_Wo': _L0_attn_in['Wo'], 'L0_attn_bo': _L0_attn_in['bo'], 'L0_ffn_ln_gamma': _L0_ffn_in['ln_gamma'], 'L0_ffn_ln_beta': _L0_ffn_in['ln_beta'], 'L0_ffn_fc1_q': _L0_ffn_in['fc1_q'], 'L0_ffn_fc1_scales': _L0_ffn_in['fc1_scales'], 'L0_ffn_fc1_bias': _L0_ffn_in['fc1_bias'], 'L0_ffn_fc2_q': _L0_ffn_in['fc2_q'], 'L0_ffn_fc2_scales': _L0_ffn_in['fc2_scales'], 'L0_ffn_fc2_bias': _L0_ffn_in['fc2_bias']}
    _x0 = _d['L0_attn_x']
    _d['L0_attn_x'] = jax.random.normal(jax.random.fold_in(jax.random.key(seed), 1), (16, 256, 128), dtype=_x0.dtype)
    del _x0
    return _d

def reference(L0_attn_x, L0_attn_Wq, L0_attn_bq, L0_attn_Wk, L0_attn_bk, L0_attn_Wv, L0_attn_bv, L0_attn_Wo, L0_attn_bo, L0_ffn_ln_gamma, L0_ffn_ln_beta, L0_ffn_fc1_q, L0_ffn_fc1_scales, L0_ffn_fc1_bias, L0_ffn_fc2_q, L0_ffn_fc2_scales, L0_ffn_fc2_bias):

    def _L0_attn_ref(x, Wq, bq, Wk, bk, Wv, bv, Wo, bo):
        import jax, jax.numpy as jnp
        import numpy as np
        N_HEADS = 16
        CHUNK = 128

        def _phi(x):
            return jax.nn.elu(x) + 1.0
        b, s, dm = x.shape
        h = N_HEADS
        d = dm // h

        def proj(W, bias):
            y = x @ W.T + bias
            return y.reshape(b, s, h, d).transpose(0, 2, 1, 3).reshape(b * h, s, d)
        q = _phi(proj(Wq, bq))
        k = _phi(proj(Wk, bk))
        v = proj(Wv, bv)
        C = CHUNK
        n = s // C
        to_chunks = lambda t: t.reshape(b * h, n, C, d).transpose(1, 0, 2, 3)
        qc, kc, vc = (to_chunks(q), to_chunks(k), to_chunks(v))
        mask = jnp.tril(jnp.ones((C, C), bool))

        def step(carry, inp):
            S, z = carry
            qi, ki, vi = inp
            scores = jnp.einsum('bqd,bkd->bqk', qi, ki)
            scores = jnp.where(mask, scores, jnp.zeros((), scores.dtype))
            num = jnp.einsum('bqk,bkd->bqd', scores, vi) + jnp.einsum('bqd,bde->bqe', qi, S)
            kcum = jnp.cumsum(ki, axis=1) + z[:, None, :]
            den = jnp.sum(qi * kcum, axis=-1, keepdims=True)
            out = num / den
            S2 = S + jnp.einsum('bkd,bke->bde', ki, vi)
            z2 = z + ki.sum(axis=1)
            return ((S2, z2), out)
        init = (jnp.zeros((b * h, d, d), x.dtype), jnp.zeros((b * h, d), x.dtype))
        _, outs = jax.lax.scan(step, init, (qc, kc, vc))
        out = outs.transpose(1, 0, 2, 3).reshape(b, h, s, d).transpose(0, 2, 1, 3).reshape(b, s, dm)
        return out @ Wo.T + bo

    def _L0_ffn_ref(x, ln_gamma, ln_beta, fc1_q, fc1_scales, fc1_bias, fc2_q, fc2_scales, fc2_bias):
        import jax, jax.numpy as jnp
        import numpy as np
        B, S, H, F, G = (8, 256, 128, 512, 128)
        EPS = 1e-05

        def _dequant(q, scales, g):
            K, N = q.shape
            w = (q.astype(jnp.float32) - 128.0).reshape(K // g, g, N) * scales[:, None, :]
            return w.reshape(K, N)
        residual = x
        mu = jnp.mean(x, axis=-1, keepdims=True)
        var = jnp.mean(jnp.square(x - mu), axis=-1, keepdims=True)
        h = (x - mu) * jax.lax.rsqrt(var + EPS) * ln_gamma + ln_beta
        hf = h.reshape(-1, H)
        w1 = _dequant(fc1_q, fc1_scales, G)
        y = hf @ w1 + fc1_bias
        y = jax.nn.silu(y)
        w2 = _dequant(fc2_q, fc2_scales, G)
        z = y @ w2 + fc2_bias
        return residual + 0.5 * z.reshape(residual.shape)
    x = L0_attn_x
    x = x + _layernorm(_L0_attn_ref(_layernorm(x, axis=-1), L0_attn_Wq, L0_attn_bq, L0_attn_Wk, L0_attn_bk, L0_attn_Wv, L0_attn_bv, L0_attn_Wo, L0_attn_bo), axis=-1)
    x = x + _layernorm(_L0_ffn_ref(_layernorm(x, axis=-1), L0_ffn_ln_gamma, L0_ffn_ln_beta, L0_ffn_fc1_q, L0_ffn_fc1_scales, L0_ffn_fc1_bias, L0_ffn_fc2_q, L0_ffn_fc2_scales, L0_ffn_fc2_bias), axis=-1)
    return x

_drawn_inputs = setup_inputs


def setup_inputs(seed=0):
    import zlib

    import numpy as np

    out = dict(_drawn_inputs(seed))
    spreads = {'L0_attn_bq': (0.0, 0.432),
     'L0_attn_bk': (0.0, 0.737),
     'L0_attn_bv': (0.0, 0.1),
     'L0_attn_bo': (0.0, 0.1),
     'L0_ffn_ln_gamma': (1.0, 0.2),
     'L0_ffn_ln_beta': (0.0, 0.1)}
    factors = {'L0_ffn_fc1_bias': 25.263, 'L0_ffn_fc2_bias': 64.0}
    for name, (base, spread) in spreads.items():
        noise = np.random.default_rng([zlib.crc32(name.encode()), seed]).standard_normal(out[name].shape)
        drawn = base * np.exp(spread * noise) if base else spread * noise
        out[name] = jnp.asarray(drawn.astype(out[name].dtype))
    for name, factor in factors.items():
        out[name] = (out[name] * factor).astype(out[name].dtype)
    return out
```

```python
from contextlib import ExitStack

import numpy as np

import concourse.bass as bass
from concourse import mybir

P = 128
D = 128
H = 16
DH = D // H
TILES = 4
GT = TILES * P
QUADS = 4
JH = H // QUADS
VT = JH * (P + DH)
EPS = 1e-5

F32 = mybir.dt.float32
I32 = mybir.dt.int32
ALU = mybir.AluOpType
ACT = mybir.ActivationFunctionType
AX_X = mybir.AxisListType.X


def build(nc, x, Wq, bq, Wk, bk, Wv, bv, Wo, bo, gamma, beta, q1, s1, b1, q2, s2, b2, out):
    NT = x.shape[0] * x.shape[1] // P
    NG = NT // TILES
    F = q1.shape[1]
    FB = F // P
    assert NG & (NG - 1) == 0 and NG >= 4 and x.shape[1] == 2 * P

    x_d = x.rearrange("b (c p) f -> p (b c) f", p=P)
    out_d = out.rearrange("b (c p) f -> p (b c) f", p=P)

    with ExitStack() as ctx:
        def sb(name, shape, dt=F32):
            return ctx.enter_context(nc.sbuf_tensor(name, shape, dt))

        def sem(name):
            return ctx.enter_context(nc.semaphore(name))

        ident = sb("ident", [P, P])
        causal = sb("causal", [P, P])
        headsel = sb("headsel", [P, H])
        blockdiag = sb("blockdiag", [P, P])
        jmask = sb("jmask", [P, JH])
        ones = sb("ones", [P, 2 * P])
        expo = sb("expo", [P, 2 * TILES])
        w_raw = sb("w_raw", [P, 4, P])
        wT = sb("wT", [P, 4, P])
        vec_rows = sb("vec_rows", [5 + FB, P])
        cols = sb("cols", [P, 5 + FB])
        bq1 = sb("bq1", [P, 2])
        bo_row = sb("bo_row", [P, D])
        b2_row = sb("b2_row", [P, D])
        b2h_row = sb("b2h_row", [P, D])
        q1_sb = sb("q1_sb", [P, F], I32)
        q2_sb = sb("q2_sb", [P, FB, D], I32)
        s1_row = sb("s1_row", [P, F])
        s2_row = sb("s2_row", [P, FB, D])
        w1 = sb("w1", [P, F])
        w2h = sb("w2h", [P, FB, D])

        x_all = sb("x_all", [P, NT * D])
        stat_x = sb("stat_x", [P, TILES, 6])
        mv_x = sb("mv_x", [P, TILES, 2])
        ve_x = sb("ve_x", [P, TILES])
        r_x = sb("r_x", [P, TILES])
        nm_x = sb("nm_x", [P, TILES])
        nb_x = sb("nb_x", [P, TILES])
        xn = sb("xn", [P, TILES, D])
        xnT = sb("xnT", [P, GT])
        k_exp = sb("k_exp", [P, GT])
        k_lin = sb("k_lin", [P, GT])
        q_exp = sb("q_exp", [P, GT])
        q_lin = sb("q_lin", [P, GT])
        kT = [sb(f"kT{i}", [P, GT]) for i in range(2)]
        qT = sb("qT", [P, GT])
        kcum = sb("kcum", [P, GT])
        qkcum = sb("qkcum", [P, GT])
        vpad = [sb(f"vpad{i}", [P, TILES, VT]) for i in range(2)]
        ktok = sb("ktok", [P, 2, D])
        state = [sb(f"state{i}", [P, 2, D]) for i in range(2)]
        rden = sb("rden", [P, TILES * H])
        rden_wide = sb("rden_wide", [P, TILES, D])
        qn = [sb(f"qn{i}", [P, GT]) for i in range(2)]
        qm = [sb(f"qm{i}", [P, TILES, JH, P]) for i in range(2)]
        sm = [sb(f"sm{i}", [P, QUADS, JH * P]) for i in range(2)]
        oT = sb("oT", [P, GT])
        a_sb = sb("a_sb", [P, TILES, D])
        stat_a = sb("stat_a", [P, TILES, 6])
        mv_a = sb("mv_a", [P, TILES, 2])
        ve_a = sb("ve_a", [P, TILES])
        r_a = sb("r_a", [P, TILES])
        mr_a = [sb(f"mr_a{i}", [P, TILES]) for i in range(2)]
        t = [sb(f"t{i}", [P, TILES, D]) for i in range(2)]
        stat_t = sb("stat_t", [P, TILES, 6])
        mv_t = sb("mv_t", [P, TILES, 2])
        ve_t = sb("ve_t", [P, 2, TILES])
        r_t = sb("r_t", [P, 2, TILES])
        nm_t = sb("nm_t", [P, TILES])
        nb_t = sb("nb_t", [P, TILES])
        z = sb("z", [P, TILES, D])
        hT = sb("hT", [P, GT])
        act_h = sb("act_h", [P, FB, GT])
        tr = sb("tr", [P, TILES, D])
        res = sb("res", [P, TILES, D])
        u = sb("u", [P, TILES, D])
        stat_u = sb("stat_u", [P, TILES, 6])
        mv_u = sb("mv_u", [P, TILES, 2])
        ve_u = sb("ve_u", [P, TILES])
        r_u = sb("r_u", [P, TILES])
        mr_u = sb("mr_u", [P, TILES])
        mr_ua = sb("mr_ua", [P, TILES])
        c_u = sb("c_u", [P, TILES])
        w_out = sb("w_out", [P, TILES, D])
        o_sb = [sb(f"o_sb{i}", [P, TILES, D]) for i in range(2)]

        bank_s = [ctx.enter_context(nc.psum_tensor(f"bank_s{g}", [P, GT], F32)) for g in range(QUADS)]
        bank_a = ctx.enter_context(nc.psum_tensor("bank_a", [P, GT], F32))
        bank_b = ctx.enter_context(nc.psum_tensor("bank_b", [P, GT], F32))
        bank_c = ctx.enter_context(nc.psum_tensor("bank_c", [P, GT], F32))
        bank_o = ctx.enter_context(nc.psum_tensor("bank_o", [P, GT], F32))

        x_here = [sem(f"x_here{i}") for i in range(3)]
        w_here = sem("w_here")
        vecs_here = sem("vecs_here")
        cols_in_psum = sem("cols_in_psum")
        cols_ready = sem("cols_ready")
        rows_here = sem("rows_here")
        scales_here = sem("scales_here")
        quants_here = sem("quants_here")
        const_step = sem("const_step")
        ident_ready = sem("ident_ready")
        masks_ready = sem("masks_ready")
        jmask_ready = sem("jmask_ready")
        zeros_ready = sem("zeros_ready")
        bias_ready = sem("bias_ready")
        w_in_psum = sem("w_in_psum")
        w_ready = sem("w_ready")
        ffn_step = sem("ffn_step")
        ffn_ready = sem("ffn_ready")

        x_stats = sem("x_stats")
        x_mv = sem("x_mv")
        x_ve = sem("x_ve")
        x_rstd = sem("x_rstd")
        x_nm = sem("x_nm")
        x_norm_ready = sem("x_norm_ready")
        xn_ready = sem("xn_ready")
        xT_in_psum = sem("xT_in_psum")
        xT_ready = sem("xT_ready")
        k_in_psum = sem("k_in_psum")
        k_read = sem("k_read")
        q_in_psum = sem("q_in_psum")
        q_read = sem("q_read")
        v_in_psum = sem("v_in_psum")
        v_ready = sem("v_ready")
        kT_ready = sem("kT_ready")
        qT_ready = sem("qT_ready")
        kcum_ready = sem("kcum_ready")
        qkcum_ready = sem("qkcum_ready")
        ktok_in_psum = sem("ktok_in_psum")
        ktok_ready = sem("ktok_ready")
        state_in_psum = sem("state_in_psum")
        state_ready = sem("state_ready")
        den_in_psum = sem("den_in_psum")
        rden_ready = sem("rden_ready")
        rden_wide_ready = sem("rden_wide_ready")
        rdT_in_psum = sem("rdT_in_psum")
        qn_ready = sem("qn_ready")
        qm_ready = sem("qm_ready")
        scores_in_psum = [[sem(f"scores_in_psum{c}{g}") for g in range(QUADS)] for c in range(TILES)]
        scores_ready = [[sem(f"scores_ready{c}{g}") for g in range(QUADS)] for c in range(TILES)]
        o_in_psum = [sem(f"o_in_psum{c}") for c in range(TILES)]
        oT_ready = sem("oT_ready")
        wo_in_psum = sem("wo_in_psum")
        a_ready = sem("a_ready")
        a_stats = sem("a_stats")
        a_mv = sem("a_mv")
        a_ve = sem("a_ve")
        a_rstd = sem("a_rstd")
        a_mr = sem("a_mr")
        t_ready = sem("t_ready")
        t_stats = sem("t_stats")
        t_mv = sem("t_mv")
        t_ve = sem("t_ve")
        t_rstd = sem("t_rstd")
        t_nm = sem("t_nm")
        t_norm_ready = sem("t_norm_ready")
        z_ready = sem("z_ready")
        hT_in_psum = sem("hT_in_psum")
        hT_ready = sem("hT_ready")
        fc1_in_psum = [sem(f"fc1_in_psum{i}") for i in range(FB)]
        act_ready = [sem(f"act_ready{i}") for i in range(FB)]
        fc2_in_psum = sem("fc2_in_psum")
        tr_ready = sem("tr_ready")
        res_ready = sem("res_ready")
        u_ready = sem("u_ready")
        u_stats = sem("u_stats")
        u_mv = sem("u_mv")
        u_ve = sem("u_ve")
        u_rstd = sem("u_rstd")
        u_mr = sem("u_mr")
        u_mra = sem("u_mra")
        u_c = sem("u_c")
        w_out_ready = sem("w_out_ready")
        o_ready = sem("o_ready")
        o_free = sem("o_free")
        stored = sem("stored")

        head_start = {e.name: 1 for e in (hT_in_psum, fc1_in_psum[FB - 1], fc2_in_psum, u_ready, u_c,
                                          w_out_ready, t_norm_ready)}
        head_start[o_ready.name] = 2
        head_start[o_free.name] = 2

        class Group:

            def __init__(self, counts, off):
                self.counts, self.off = counts, off

            def __add__(self, n):
                return Group(self.counts, self.off + n)

            def __sub__(self, n):
                return Group(self.counts, self.off - n)

            def count(self):
                return self.counts[self.off]

        def after(eng, event, G):
            ahead = head_start.get(event.name, 0)
            if isinstance(G, int):
                if G >= 0:
                    eng.wait_ge(event, G + 1 + ahead)
            else:
                assert (G + 1 + ahead).off > -2, event.name
                eng.wait_ge(event, (G + 1 + ahead).count())

        def apart(eng):
            eng.wait_ge(ident_ready, 1)

        def steps(eng, step):
            step(0, 0)
            step(1, 1)
            with eng.Fori(1, NG // 2) as turn:
                counts = {off: eng.snap(turn * 2 + off) for off in range(-2, 4)}
                for count in counts.values():
                    eng.compute_val(count)
                step(Group(counts, 0), 0)
                step(Group(counts, 1), 1)
            step(NG, 0)
            step(NG + 1, 1)

        def comes_next(s):
            return not isinstance(s, int) or s + 1 < NG

        def x_tile(G, c):
            if isinstance(G, int):
                return x_all[:, G * GT + c * D:G * GT + (c + 1) * D]
            g = G.count() if G.off < 2 else G.count() & (NG - 1)
            return x_all[:, bass.ds(g * GT + c * D, D)]

        def has(s):
            if isinstance(s, int):
                return s < NG, 1 <= s <= NG, s >= 2
            return True, True, True

        block = ctx.enter_context(nc.Block())

        @block.sync
        def _(sp):
            def load_x(g0, g1, s_here):
                sp.dma_start(x_all[:, g0 * GT:g1 * GT].rearrange("p (t f) -> p t f", f=D),
                             x_d[:, g0 * TILES:g1 * TILES, :]).then_inc(s_here, 16)
            load_x(0, 1, x_here[0])
            for i, w in enumerate((Wq, Wk, Wv, Wo)):
                sp.dma_start(w_raw[:, i, :], w).then_inc(w_here, 16)
            load_x(1, 2, x_here[1])
            load_x(2, NG, x_here[2])
            for e in (hT_in_psum, fc1_in_psum[FB - 1], fc2_in_psum, u_ready, u_c, w_out_ready,
                      t_norm_ready, o_ready, o_free):
                sp.sem_inc(e, head_start[e.name])

            def store(s, p):
                if not has(s)[2]:
                    return
                G = s - 2
                after(sp, o_ready, G)
                if isinstance(G, int):
                    dst = out_d[:, G * TILES:(G + 1) * TILES, :]
                else:
                    dst = out_d[:, bass.ds(G.count() * TILES, TILES), :]
                sp.dma_start(dst, o_sb[p][:]).then_inc(stored, 16)
                sp.wait_ge(stored, 16 * (G + 1) if isinstance(G, int) else (G + 1).count() * 16)
                sp.sem_inc(o_free, 1)
            steps(sp, store)

        @block.gpsimd
        def _(pool):
            for v, dst in ((s1[0], s1_row[:]), (s2.rearrange("k n -> (k n)"), s2_row[:].rearrange("p k n -> p (k n)"))):
                pool.dma_start(dst, v.partition_broadcast(P)).then_inc(scales_here, 16)
            for v, dst in ((bo, bo_row), (b2, b2_row)):
                pool.dma_start(dst[:], v.partition_broadcast(P)).then_inc(rows_here, 16)
            nc.gpsimd.memset(ident[:], 0.0).then_inc(const_step, 1)
            nc.gpsimd.memset(causal[:], 1.0).then_inc(const_step, 1)
            nc.gpsimd.memset(headsel[:], 1.0).then_inc(const_step, 1)
            nc.gpsimd.memset(expo[:], -0.5).then_inc(const_step, 1)
            nc.gpsimd.memset(ones[:], 1.0).then_inc(const_step, 1)
            pool.wait_ge(const_step, 5)
            nc.gpsimd.affine_select(out=ident[:], in_=ident[:], compare_op=ALU.not_equal, fill=1.0, base=0,
                                    pattern=[[-1, P]], channel_multiplier=1).then_inc(ident_ready, 1)
            nc.gpsimd.affine_select(out=causal[:], in_=causal[:], compare_op=ALU.is_ge, fill=0.0, base=0,
                                    pattern=[[1, P]], channel_multiplier=-1).then_inc(masks_ready, 1)
            nc.gpsimd.affine_select(out=headsel[:], in_=headsel[:], compare_op=ALU.is_ge, fill=0.0, base=0,
                                    pattern=[[-DH, H]], channel_multiplier=1).then_inc(const_step, 1)
            pool.wait_ge(const_step, 6)
            nc.gpsimd.affine_select(out=headsel[:], in_=headsel[:], compare_op=ALU.is_ge, fill=0.0, base=DH - 1,
                                    pattern=[[DH, H]], channel_multiplier=-1).then_inc(masks_ready, 1)

            def scale_x(G):
                apart(pool)
                after(pool, x_mv, G)
                after(pool, xn_ready, G - 1)
                nc.gpsimd.tensor_scalar(ve_x[:], mv_x[:, :, 1], 1.0, EPS, ALU.mult, ALU.add).then_inc(x_ve, 1)
                nc.gpsimd.tensor_scalar(nm_x[:], mv_x[:, :, 0], -1.0, 1.0, ALU.mult, ALU.mult).then_inc(x_nm, 1)
                after(pool, x_ve, G)
                nc.gpsimd.tensor_tensor(r_x[:], ve_x[:], expo[:, 0:TILES], ALU.pow).then_inc(x_rstd, 1)
                after(pool, x_rstd, G)
                after(pool, x_nm, G)
                nc.gpsimd.tensor_tensor(nb_x[:], nm_x[:], r_x[:], ALU.mult).then_inc(x_norm_ready, 1)

            scale_x(0)

            def step(s, p):
                P_, S_, F_ = has(s)
                if F_:
                    G, pf = s - 2, p
                    apart(pool)
                    after(pool, t_mv, G)
                    nc.gpsimd.tensor_scalar(ve_t[:, 0, :], mv_t[:, :, 1], 1.0, EPS, ALU.mult, ALU.add)
                    nc.gpsimd.tensor_scalar(ve_t[:, 1, :], mv_t[:, :, 1], 1.0 + EPS, EPS * EPS, ALU.mult,
                                            ALU.add).then_inc(t_ve, 1)
                    nc.gpsimd.tensor_scalar(nm_t[:], mv_t[:, :, 0], -1.0, 1.0, ALU.mult, ALU.mult).then_inc(t_nm, 1)
                    after(pool, t_ve, G)
                    nc.gpsimd.tensor_tensor(r_t[:].rearrange("p a t -> p (a t)"),
                                            ve_t[:].rearrange("p a t -> p (a t)"), expo[:], ALU.pow).then_inc(t_rstd, 1)
                    after(pool, t_rstd, G)
                    after(pool, t_nm, G)
                    nc.gpsimd.tensor_tensor(nb_t[:], nm_t[:], r_t[:, 1, :], ALU.mult).then_inc(t_norm_ready, 1)
                    if isinstance(G, int) and G == 0:
                        pool.wait_ge(ffn_ready, 1)
                    apart(pool)
                    after(pool, u_ready, G - 1)
                    after(pool, t_ready, G)
                    for c in range(TILES):
                        i = nc.gpsimd.tensor_scalar(tr[:, c, :], t[pf][:, c, :], r_t[:, 0, c:c + 1], 1.0,
                                                    ALU.mult, ALU.mult)
                    i.then_inc(tr_ready, 1)
                    after(pool, tr_ready, G)
                    nc.gpsimd.tensor_tensor(res[:], tr[:], b2h_row[:, None, :].to_broadcast([P, TILES, D]),
                                            ALU.add).then_inc(res_ready, 1)
                if P_:
                    G = s
                    after(pool, kcum_ready, G)
                    after(pool, qT_ready, G)
                    after(pool, den_in_psum, G - 1)
                    nc.gpsimd.tensor_tensor(qkcum[:], qT[:], kcum[:], ALU.mult).then_inc(qkcum_ready, 1)
                if comes_next(s):
                    scale_x(s + 1)
                if S_:
                    G, ps = s - 1, 1 - p
                    apart(pool)
                    after(pool, a_mv, G)
                    nc.gpsimd.tensor_scalar(ve_a[:], mv_a[:, :, 1], 1.0, EPS, ALU.mult, ALU.add).then_inc(a_ve, 1)
                    after(pool, a_ve, G)
                    nc.gpsimd.tensor_tensor(r_a[:], ve_a[:], expo[:, 0:TILES], ALU.pow).then_inc(a_rstd, 1)
                    after(pool, a_rstd, G)
                    nc.gpsimd.tensor_tensor(mr_a[ps][:], mv_a[:, :, 0], r_a[:], ALU.mult).then_inc(a_mr, 1)
                if F_:
                    G, pf = s - 2, p
                    apart(pool)
                    after(pool, u_mv, G)
                    nc.gpsimd.tensor_scalar(ve_u[:], mv_u[:, :, 1], 1.0, EPS, ALU.mult, ALU.add).then_inc(u_ve, 1)
                    after(pool, u_ve, G)
                    nc.gpsimd.tensor_tensor(r_u[:], ve_u[:], expo[:, 0:TILES], ALU.pow).then_inc(u_rstd, 1)
                    after(pool, u_rstd, G)
                    nc.gpsimd.tensor_tensor(mr_u[:], mv_u[:, :, 0], r_u[:], ALU.mult).then_inc(u_mr, 1)
                    after(pool, u_mr, G)
                    nc.gpsimd.tensor_tensor(mr_ua[:], mr_u[:], mr_a[pf][:], ALU.add).then_inc(u_mra, 1)
                    apart(pool)
                    after(pool, u_mra, G)
                    nc.gpsimd.tensor_scalar(c_u[:], mr_ua[:], -1.0, 1.0, ALU.mult, ALU.mult).then_inc(u_c, 1)
                    apart(pool)
                    after(pool, u_c, G)
                    for c in range(TILES):
                        i = nc.gpsimd.tensor_scalar(w_out[:, c, :], u[:, c, :], r_u[:, c:c + 1], c_u[:, c:c + 1],
                                                    ALU.mult, ALU.add)
                    i.then_inc(w_out_ready, 1)
                    after(pool, w_out_ready, G)
                    after(pool, o_free, G - 2)
                    nc.gpsimd.tensor_tensor(o_sb[p][:], w_out[:], t[pf][:], ALU.add).then_inc(o_ready, 1)
            steps(pool, step)

        @block.scalar
        def _(act):
            for i, v in enumerate((bq, bk, bv, gamma, beta)):
                act.dma_start(vec_rows[i:i + 1, :], v[None, :]).then_inc(vecs_here, 16)
            act.dma_start(vec_rows[5:5 + FB, :], b1.rearrange("(k p) -> k p", p=P)).then_inc(vecs_here, 16)
            act.dma_start(q1_sb[:], q1).then_inc(quants_here, 16)
            act.dma_start(q2_sb[:], q2.rearrange("(k p) n -> p k n", p=P)).then_inc(quants_here, 16)

            def normalise_x(G):
                after(act, x_norm_ready, G)
                after(act, xT_in_psum, G - 1)
                for c in range(TILES):
                    i = nc.scalar.activation(xn[:, c, :], x_tile(G, c), ACT.Identity, bias=nb_x[:, c:c + 1],
                                             scale=r_x[:, c:c + 1])
                i.then_inc(xn_ready, 1)

            def silu(s, i):
                G = s - 2
                if i == 0:
                    after(act, fc2_in_psum, G - 1)
                after(act, fc1_in_psum[i], G)
                nc.scalar.activation(act_h[:, i, :], (bank_a if i % 2 == 0 else bank_b)[:], ACT.Silu,
                                     bias=cols[:, 5 + i:6 + i]).then_inc(act_ready[i], 1)

            normalise_x(0)
            act.wait_ge(w_in_psum, 1)
            nc.scalar.activation(wT[:].rearrange("p k n -> p (k n)"), bank_a[:], ACT.Copy).then_inc(w_ready, 1)
            act.wait_ge(cols_in_psum, 1)
            nc.scalar.activation(cols[:], bank_b[:, 0:5 + FB], ACT.Copy).then_inc(cols_ready, 1)
            act.wait_ge(cols_ready, 1)

            def step(s, p):
                P_, S_, F_ = has(s)
                if P_:
                    G = s
                    after(act, xT_in_psum, G)
                    after(act, v_in_psum, G - 1)
                    nc.scalar.activation(xnT[:], bank_a[:], ACT.Copy).then_inc(xT_ready, 1)
                    after(act, k_in_psum, G)
                    after(act, kT_ready, G - 1)
                    nc.scalar.activation(k_exp[:], bank_a[:], ACT.Exp, bias=cols[:, 1:2])
                    if isinstance(G, int) and G == 0:
                        act.wait_ge(bias_ready, 1)
                    nc.scalar.activation(k_lin[:], bank_a[:], ACT.Identity, bias=bq1[:, 1:2]).then_inc(k_read, 1)
                    after(act, q_in_psum, G)
                    after(act, qT_ready, G - 1)
                    nc.scalar.activation(q_exp[:], bank_b[:], ACT.Exp, bias=cols[:, 0:1])
                    nc.scalar.activation(q_lin[:], bank_b[:], ACT.Identity, bias=bq1[:, 0:1]).then_inc(q_read, 1)
                    after(act, v_in_psum, G)
                    if isinstance(G, int) and G < 2:
                        act.wait_ge(zeros_ready, G + 1)
                    after(act, o_in_psum[TILES - 1], G - 2)
                    for c in range(TILES):
                        dst = vpad[p][:, c, :].rearrange("p (j r) -> p j r", j=JH)[:, :, 0:P]
                        dst = dst.rearrange("p j (g r) -> p j g r", g=QUADS)[:, :, :, 0:DH]
                        dst = dst.rearrange("p j g e -> p g j e")
                        src = bank_b[:, c * P:(c + 1) * P].rearrange("p (g j e) -> p g j e", g=QUADS, j=JH)
                        i = nc.scalar.activation(dst, src, ACT.Copy)
                    i.then_inc(v_ready, 1)
                if F_:
                    G, pf = s - 2, p
                    after(act, t_norm_ready, G)
                    after(act, t_ready, G)
                    after(act, hT_in_psum, G - 1)
                    for c in range(TILES):
                        i = nc.scalar.activation(z[:, c, :], t[pf][:, c, :], ACT.Identity, bias=nb_t[:, c:c + 1],
                                                 scale=r_t[:, 1, c:c + 1])
                    i.then_inc(z_ready, 1)
                    after(act, hT_in_psum, G)
                    after(act, fc1_in_psum[FB - 1], G - 1)
                    nc.scalar.activation(hT[:], bank_c[:], ACT.Identity, bias=cols[:, 4:5],
                                         scale=cols[:, 3:4]).then_inc(hT_ready, 1)
                if P_:
                    G = s
                    after(act, ktok_in_psum, G)
                    after(act, state_in_psum, G - 1)
                    nc.scalar.activation(ktok[:].rearrange("p b f -> p (b f)"), bank_c[:, 0:2 * D],
                                         ACT.Copy).then_inc(ktok_ready, 1)
                if comes_next(s):
                    normalise_x(s + 1)
                if F_:
                    silu(s, 0)
                    silu(s, 1)
                if S_:
                    G = s - 1
                    after(act, o_in_psum[TILES - 1], G)
                    after(act, wo_in_psum, G - 1)
                    nc.scalar.activation(oT[:], bank_o[:], ACT.Identity, bias=cols[:, 2:3]).then_inc(oT_ready, 1)
                if F_:
                    silu(s, 2)
                if P_:
                    G = s
                    after(act, rden_ready, G)
                    after(act, rdT_in_psum, G - 1)
                    nc.scalar.activation(rden_wide[:].rearrange("p t (h e) -> p (t h) e", e=DH),
                                         rden[:, :, None].to_broadcast([P, TILES * H, DH]),
                                         ACT.Copy).then_inc(rden_wide_ready, 1)
                if F_:
                    silu(s, 3)
                if P_:
                    G = s
                    if isinstance(G, int) and G == 0:
                        act.wait_ge(jmask_ready, 1)
                    after(act, qn_ready, G)
                    after(act, scores_in_psum[TILES - 1][QUADS - 1], G - 2)
                    for j in range(JH):
                        i = nc.scalar.activation(qm[p][:, :, j, :], qn[p][:].rearrange("p (t q) -> p t q", q=P),
                                                 ACT.Copy, scale=jmask[:, j:j + 1])
                    i.then_inc(qm_ready, 1)
            steps(act, step)

        @block.vector
        def _(dve):
            def moments(src, stat, mv, s_stat, s_mv, G):
                for c in range(TILES):
                    i = nc.vector.bn_stats(stat[:, c, :], src(c))
                i.then_inc(s_stat, 1)
                apart(dve)
                after(dve, s_stat, G)
                for c in range(TILES):
                    i = nc.vector.bn_aggr(mv[:, c, :], stat[:, c, :])
                i.then_inc(s_mv, 1)

            def mask_scores(s, p, c):
                G = s - 1
                for g in range(QUADS):
                    after(dve, scores_in_psum[c][g], G)
                    if g == 0:
                        if c < 2:
                            after(dve, o_in_psum[c + 2], G - 1)
                        else:
                            after(dve, o_in_psum[c - 2], G)
                    nc.vector.tensor_tensor(sm[c % 2][:, g, :].rearrange("p (j q) -> p j q", j=JH),
                                            bank_s[g][:].rearrange("p (j q) -> p j q", j=JH),
                                            causal[:, None, :].to_broadcast([P, JH, P]),
                                            ALU.mult).then_inc(scores_ready[c][g], 1)

            def setup_ffn():
                dve.wait_ge(quants_here, 32)
                dve.wait_ge(scales_here, 32)
                nc.vector.tensor_scalar(w1[:], q1_sb[:], -128.0, None, ALU.add).then_inc(ffn_step, 1)
                nc.vector.tensor_scalar(w2h[:], q2_sb[:], -128.0, 0.5, ALU.add, ALU.mult).then_inc(ffn_step, 1)
                dve.wait_ge(ffn_step, 2)
                nc.vector.tensor_tensor(w1[:], w1[:], s1_row[:], ALU.mult)
                nc.vector.tensor_tensor(w2h[:], w2h[:], s2_row[:], ALU.mult)
                dve.wait_ge(rows_here, 32)
                nc.vector.tensor_scalar(b2h_row[:], b2_row[:], 0.5, None, ALU.mult).then_inc(ffn_ready, 1)

            def stats_x(G):
                if isinstance(G, int) and G < 3:
                    dve.wait_ge(x_here[G], 16)
                after(dve, x_norm_ready, G - 1)
                moments(lambda c: x_tile(G, c), stat_x, mv_x, x_stats, x_mv, G)

            stats_x(0)

            def step(s, p):
                P_, S_, F_ = has(s)
                first = isinstance(s, int) and s == 0
                if first:
                    dve.wait_ge(cols_ready, 1)
                    nc.vector.tensor_scalar(bq1[:], cols[:, 0:2], 1.0, None, ALU.add).then_inc(bias_ready, 1)
                    nc.vector.memset(vpad[0][:], 0.0).then_inc(zeros_ready, 1)
                    dve.wait_ge(masks_ready, 2)
                    nc.vector.tensor_copy(blockdiag[:].rearrange("p (h e) -> p h e", e=DH),
                                          headsel[:, :, None].to_broadcast([P, H, DH]))
                    nc.vector.tensor_reduce(jmask[:], headsel[:].rearrange("p (g j) -> p j g", g=QUADS), AX_X,
                                            ALU.add).then_inc(jmask_ready, 1)
                if F_:
                    G, pf = s - 2, p
                    after(dve, a_rstd, G)
                    after(dve, o_ready, G - 2)
                    for c in range(TILES):
                        i = nc.vector.scalar_tensor_tensor(t[pf][:, c, :], a_sb[:, c, :], r_a[:, c:c + 1],
                                                           x_tile(G, c), ALU.mult, ALU.add)
                    i.then_inc(t_ready, 1)
                    after(dve, t_ready, G)
                    after(dve, t_norm_ready, G - 1)
                    moments(lambda c: t[pf][:, c, :], stat_t, mv_t, t_stats, t_mv, G)
                if S_:
                    mask_scores(s, p, 0)
                    mask_scores(s, p, 1)
                if P_:
                    G = s
                    after(dve, k_read, G)
                    after(dve, scores_in_psum[TILES - 1][QUADS - 1], G - 2)
                    nc.vector.scalar_tensor_tensor(kT[p][:], k_exp[:], 1.0, k_lin[:], ALU.min, ALU.max).then_inc(kT_ready, 1)
                    after(dve, q_read, G)
                    after(dve, qkcum_ready, G - 1)
                    nc.vector.scalar_tensor_tensor(qT[:], q_exp[:], 1.0, q_lin[:], ALU.min, ALU.max).then_inc(qT_ready, 1)
                    after(dve, kT_ready, G)
                    for b in range(2):
                        cut = slice(b * 2 * P, (b + 1) * 2 * P)
                        i = nc.vector.tensor_tensor_scan(kcum[:, cut], ones[:], kT[p][:, cut], 0.0, ALU.mult, ALU.add)
                    i.then_inc(kcum_ready, 1)
                if first:
                    nc.vector.memset(vpad[1][:], 0.0).then_inc(zeros_ready, 1)
                if S_:
                    mask_scores(s, p, 2)
                if comes_next(s):
                    stats_x(s + 1)
                if first:
                    setup_ffn()
                if S_:
                    mask_scores(s, p, 3)
                if P_:
                    G = s
                    after(dve, state_in_psum, G)
                    after(dve, o_in_psum[TILES - 1], G - 2)
                    nc.vector.tensor_tensor(state[p][:], bank_c[:, 0:2 * D].rearrange("p (b f) -> p b f", b=2),
                                            blockdiag[:, None, :].to_broadcast([P, 2, D]), ALU.mult).then_inc(state_ready, 1)
                    after(dve, den_in_psum, G)
                    after(dve, rden_wide_ready, G - 1)
                    nc.vector.reciprocal(rden[:], bank_c[:, 0:TILES * H]).then_inc(rden_ready, 1)
                if S_:
                    G = s - 1
                    after(dve, wo_in_psum, G)
                    after(dve, t_ready, G - 1)
                    nc.vector.tensor_tensor(a_sb[:], bank_c[:].rearrange("p (t f) -> p t f", f=D),
                                            bo_row[:, None, :].to_broadcast([P, TILES, D]), ALU.add).then_inc(a_ready, 1)
                if P_:
                    G = s
                    after(dve, rdT_in_psum, G)
                    after(dve, o_in_psum[TILES - 1], G - 2)
                    nc.vector.tensor_tensor(qn[p][:], bank_a[:], qT[:], ALU.mult).then_inc(qn_ready, 1)
                if S_:
                    G = s - 1
                    after(dve, a_ready, G)
                    after(dve, a_mr, G - 1)
                    moments(lambda c: a_sb[:, c, :], stat_a, mv_a, a_stats, a_mv, G)
                if F_:
                    G = s - 2
                    after(dve, fc2_in_psum, G)
                    after(dve, res_ready, G)
                    after(dve, w_out_ready, G - 1)
                    nc.vector.tensor_tensor(u[:].rearrange("p t f -> p (t f)"), bank_b[:],
                                            res[:].rearrange("p t f -> p (t f)"), ALU.add).then_inc(u_ready, 1)
                    after(dve, u_ready, G)
                    after(dve, u_c, G - 1)
                    moments(lambda c: u[:, c, :], stat_u, mv_u, u_stats, u_mv, G)
            steps(dve, step)

        @block.tensor
        def _(pe):
            pe.wait_ge(ident_ready, 1)
            pe.wait_ge(w_here, 64)
            for i in range(4):
                last = nc.tensor.transpose(bank_a[:, i * P:(i + 1) * P], w_raw[:, i, :], ident[:])
            last.then_inc(w_in_psum, 1)
            pe.wait_ge(vecs_here, 96)
            nc.tensor.transpose(bank_b[:, 0:5 + FB], vec_rows[:], ident[0:5 + FB, 0:5 + FB]).then_inc(cols_in_psum, 1)
            WQ, WK, WV, WO = (wT[:, i, :] for i in range(4))

            def tile(c):
                return slice(c * P, (c + 1) * P)

            def scores(s, p, c):
                G, ps = s - 1, 1 - p
                if c == 0:
                    after(pe, qm_ready, G)
                for g in range(QUADS):
                    if c == 0:
                        after(pe, scores_ready[TILES - 1][g], G - 1)
                    else:
                        after(pe, scores_ready[c - 1][g], G)
                    rows = slice(32 * g, 32 * g + 32)
                    nc.tensor.matmul(bank_s[g][:], kT[ps][rows, tile(c)],
                                     qm[ps][rows, c, :, :].rearrange("p j q -> p (j q)"),
                                     start=True, stop=True).then_inc(scores_in_psum[c][g], 1)

            def numerators(s, p, c):
                G, ps = s - 1, 1 - p
                if c == 0:
                    after(pe, oT_ready, G - 1)
                after_state = c % 2 == 1
                if after_state:
                    nc.tensor.matmul(bank_o[:, tile(c)], state[ps][:, c // 2, :], qn[ps][:, tile(c)],
                                     start=True, stop=False, skip_group_check=True)
                for g in range(QUADS):
                    after(pe, scores_ready[c][g], G)
                for j in range(JH):
                    for g in range(QUADS):
                        last = nc.tensor.matmul(bank_o[32 * g:32 * g + 32, tile(c)],
                                                vpad[ps][:, c, j * P + 32 * g:j * P + 32 * g + 32],
                                                sm[c % 2][:, g, tile(j)],
                                                start=j == 0 and not after_state, stop=j == JH - 1,
                                                skip_group_check=True)
                last.then_inc(o_in_psum[c], 1)

            def fc1(s, i):
                G = s - 2
                nc.tensor.matmul((bank_a if i % 2 == 0 else bank_b)[:], w1[:, tile(i)], hT[:],
                                 start=True, stop=True).then_inc(fc1_in_psum[i], 1)

            def step(s, p):
                P_, S_, F_ = has(s)
                if S_:
                    scores(s, p, 0)
                if P_:
                    G = s
                    after(pe, xn_ready, G)
                    after(pe, qn_ready, G - 1)
                    if isinstance(G, int) and G == 0:
                        pe.wait_ge(w_ready, 1)
                    for c in range(TILES):
                        last = nc.tensor.transpose(bank_a[:, tile(c)], xn[:, c, :], ident[:])
                    last.then_inc(xT_in_psum, 1)
                if S_:
                    scores(s, p, 1)
                if P_:
                    G = s
                    after(pe, xT_ready, G)
                    nc.tensor.matmul(bank_a[:], WK, xnT[:], start=True, stop=True).then_inc(k_in_psum, 1)
                    after(pe, u_ready, G - 3)
                    if isinstance(G, int) and G == 0:
                        pe.wait_ge(cols_ready, 1)
                    nc.tensor.matmul(bank_b[:], WQ, xnT[:], start=True, stop=True).then_inc(q_in_psum, 1)
                if S_:
                    numerators(s, p, 0)
                    scores(s, p, 2)
                if P_:
                    G = s
                    after(pe, q_read, G)
                    for c in range(TILES):
                        last = nc.tensor.matmul(bank_b[:, tile(c)], xnT[:, tile(c)], WV, start=True, stop=True)
                    last.then_inc(v_in_psum, 1)
                if S_:
                    numerators(s, p, 1)
                if F_:
                    G = s - 2
                    after(pe, z_ready, G)
                    after(pe, a_ready, G)
                    for c in range(TILES):
                        last = nc.tensor.transpose(bank_c[:, tile(c)], z[:, c, :], ident[:])
                    last.then_inc(hT_in_psum, 1)
                if S_:
                    scores(s, p, 3)
                if P_:
                    G = s
                    after(pe, kT_ready, G)
                    after(pe, hT_ready, G - 2)
                    if isinstance(G, int) and G == 1:
                        after(pe, rden_ready, 0)
                    for b in range(2):
                        last = nc.tensor.transpose(bank_c[:, tile(b)], kT[p][:, tile(2 * b)], ident[:])
                    last.then_inc(ktok_in_psum, 1)
                if S_:
                    numerators(s, p, 2)
                if F_:
                    G = s - 2
                    if P_:
                        after(pe, k_read, s)
                        after(pe, v_ready, s)
                    else:
                        after(pe, qn_ready, NG - 1)
                        after(pe, u_ready, G - 1)
                    if isinstance(G, int) and G == 0:
                        pe.wait_ge(ffn_ready, 1)
                    after(pe, hT_ready, G)
                    fc1(s, 0)
                    fc1(s, 1)
                if P_:
                    G = s
                    after(pe, ktok_ready, G)
                    after(pe, v_ready, G)
                    for b in range(2):
                        v_rows = vpad[p][:, 2 * b, :].rearrange("p (j r) -> p j r", j=JH)[:, :, 0:P]
                        v_rows = v_rows.rearrange("p j (g r) -> p j g r", g=QUADS)[:, :, :, 0:DH]
                        last = nc.tensor.matmul(bank_c[:, tile(b)], ktok[:, b, :],
                                                v_rows.rearrange("p j g e -> p g j e"), start=True, stop=True)
                    last.then_inc(state_in_psum, 1)
                if S_:
                    numerators(s, p, 3)
                if F_:
                    after(pe, act_ready[0], s - 2)
                    fc1(s, 2)
                if P_:
                    G = s
                    after(pe, qkcum_ready, G)
                    after(pe, state_ready, G)
                    for c in range(TILES):
                        last = nc.tensor.matmul(bank_c[:, c * H:(c + 1) * H], qkcum[:, tile(c)], headsel[:],
                                                start=True, stop=True)
                    last.then_inc(den_in_psum, 1)
                if F_:
                    after(pe, act_ready[1], s - 2)
                    fc1(s, 3)
                if S_:
                    G = s - 1
                    after(pe, oT_ready, G)
                    if P_:
                        after(pe, rden_ready, s)
                    else:
                        after(pe, hT_ready, s - 2)
                    for c in range(TILES):
                        last = nc.tensor.matmul(bank_c[:, tile(c)], oT[:, tile(c)], WO, start=True, stop=True)
                    last.then_inc(wo_in_psum, 1)
                if P_:
                    G = s
                    if F_:
                        after(pe, act_ready[2], s - 2)
                    else:
                        after(pe, k_read, G)
                    after(pe, rden_wide_ready, G)
                    for c in range(TILES):
                        last = nc.tensor.matmul(bank_a[:, tile(c)], rden_wide[:, c, :],
                                                ident[:], start=True, stop=True, is_transpose=True)
                    last.then_inc(rdT_in_psum, 1)
                if F_:
                    G = s - 2
                    after(pe, act_ready[FB - 1], G)
                    for c in range(TILES):
                        for i in range(FB):
                            last = nc.tensor.matmul(bank_b[:, tile(c)], act_h[:, i, tile(c)], w2h[:, i, :],
                                                    start=i == 0, stop=i == FB - 1)
                    last.then_inc(fc2_in_psum, 1)
            steps(pe, step)


_INS = ['L0_attn_x', 'L0_attn_Wq', 'L0_attn_bq', 'L0_attn_Wk', 'L0_attn_bk', 'L0_attn_Wv', 'L0_attn_bv',
        'L0_attn_Wo', 'L0_attn_bo', 'L0_ffn_ln_gamma', 'L0_ffn_ln_beta', 'L0_ffn_fc1_q', 'L0_ffn_fc1_scales',
        'L0_ffn_fc1_bias', 'L0_ffn_fc2_q', 'L0_ffn_fc2_scales', 'L0_ffn_fc2_bias']


def kernel(**inputs):
    import concourse.bacc as bacc
    from concourse.bass_utils import run_bass_kernel_spmd

    nc = bacc.Bacc("TRN2", target_bir_lowering=False, num_devices=1)
    arrays, args = {}, []
    for name in _INS:
        a = np.ascontiguousarray(inputs[name])
        arrays[name] = a
        args.append(nc.dram_tensor(name, a.shape, mybir.dt.from_np(a.dtype), kind="ExternalInput").ap())
    shape = arrays['L0_attn_x'].shape
    args.append(nc.dram_tensor("y", shape, F32, kind="ExternalOutput").ap())
    build(nc, *args)
    return run_bass_kernel_spmd(nc, [arrays], core_ids=[0]).results[0]["y"]
```

```python
from contextlib import ExitStack

import numpy as np

import concourse.bass as bass
from concourse import mybir

P = 128
D = 128
H = 16
DH = D // H
TILES = 4
GT = TILES * P
QUADS = 4
JH = H // QUADS
VT = JH * (P + DH)
PARTS = [(c, g) for c in range(TILES) for g in range(QUADS)]
QM_ACT = 1
EPS = 1e-5

F32 = mybir.dt.float32
I32 = mybir.dt.int32
ALU = mybir.AluOpType
ACT = mybir.ActivationFunctionType
AX_X = mybir.AxisListType.X


def build(nc, x, Wq, bq, Wk, bk, Wv, bv, Wo, bo, gamma, beta, q1, s1, b1, q2, s2, b2, out):
    NT = x.shape[0] * x.shape[1] // P
    NG = NT // TILES
    F = q1.shape[1]
    FB = F // P
    assert NG & (NG - 1) == 0 and NG >= 4 and x.shape[1] == 2 * P

    x_d = x.rearrange("b (c p) f -> p (b c) f", p=P)
    out_d = out.rearrange("b (c p) f -> p (b c) f", p=P)

    with ExitStack() as ctx:
        def sb(name, shape, dt=F32):
            return ctx.enter_context(nc.sbuf_tensor(name, shape, dt))

        def sem(name):
            return ctx.enter_context(nc.semaphore(name))

        ident = sb("ident", [P, P])
        causal = sb("causal", [P, P])
        headsel = sb("headsel", [P, H])
        blockdiag = sb("blockdiag", [P, P])
        jmask = sb("jmask", [P, JH])
        ones = sb("ones", [P, 2 * P])
        scrap = sb("scrap", [P, 1])
        expo = sb("expo", [P, 2 * TILES])
        w_raw = sb("w_raw", [P, 4, P])
        wT = sb("wT", [P, 4, P])
        vec_rows = sb("vec_rows", [5 + FB, P])
        cols = sb("cols", [P, 5 + FB])
        bq1 = sb("bq1", [P, 2])
        bo_row = sb("bo_row", [P, D])
        b2_row = sb("b2_row", [P, D])
        b2h_row = sb("b2h_row", [P, D])
        q1_sb = sb("q1_sb", [P, F], I32)
        q2_sb = sb("q2_sb", [P, FB, D], I32)
        s1_row = sb("s1_row", [P, F])
        s2_row = sb("s2_row", [P, FB, D])
        w1 = sb("w1", [P, F])
        w2h = sb("w2h", [P, FB, D])

        x_all = sb("x_all", [P, NT * D])
        stat_x = sb("stat_x", [P, TILES, 6])
        mv_x = sb("mv_x", [P, TILES, 2])
        ve_x = sb("ve_x", [P, TILES])
        r_x = sb("r_x", [P, TILES])
        nm_x = sb("nm_x", [P, TILES])
        nb_x = sb("nb_x", [P, TILES])
        xn = sb("xn", [P, TILES, D])
        xnT = sb("xnT", [P, GT])
        k_exp = sb("k_exp", [P, GT])
        k_lin = sb("k_lin", [P, GT])
        q_exp = sb("q_exp", [P, GT])
        q_lin = sb("q_lin", [P, GT])
        kT = [sb(f"kT{i}", [P, GT]) for i in range(2)]
        qT = sb("qT", [P, GT])
        kcum = sb("kcum", [P, GT])
        qkcum = sb("qkcum", [P, GT])
        vpad = [sb(f"vpad{i}", [P, TILES, VT]) for i in range(2)]
        ktok = sb("ktok", [P, 2, D])
        state = [sb(f"state{i}", [P, 2, D]) for i in range(2)]
        rden = sb("rden", [P, TILES * H])
        rden_wide = sb("rden_wide", [P, TILES, D])
        qn = [sb(f"qn{i}", [P, GT]) for i in range(2)]
        qm = [sb(f"qm{i}", [P, TILES, JH, P]) for i in range(2)]
        sm = [sb(f"sm{i}", [P, QUADS, JH * P]) for i in range(2)]
        oT = sb("oT", [P, GT])
        a_sb = sb("a_sb", [P, TILES, D])
        stat_a = sb("stat_a", [P, TILES, 6])
        mv_a = sb("mv_a", [P, TILES, 2])
        ve_a = sb("ve_a", [P, TILES])
        r_a = sb("r_a", [P, TILES])
        mr_a = [sb(f"mr_a{i}", [P, TILES]) for i in range(2)]
        t = [sb(f"t{i}", [P, TILES, D]) for i in range(2)]
        stat_t = sb("stat_t", [P, TILES, 6])
        mv_t = sb("mv_t", [P, TILES, 2])
        ve_t = sb("ve_t", [P, 2, TILES])
        r_t = sb("r_t", [P, 2, TILES])
        nm_t = sb("nm_t", [P, TILES])
        nb_t = sb("nb_t", [P, TILES])
        z = sb("z", [P, TILES, D])
        hT = sb("hT", [P, GT])
        act_h = sb("act_h", [P, FB, GT])
        tr = sb("tr", [P, TILES, D])
        res = sb("res", [P, TILES, D])
        u = sb("u", [P, TILES, D])
        stat_u = sb("stat_u", [P, TILES, 6])
        mv_u = sb("mv_u", [P, TILES, 2])
        ve_u = sb("ve_u", [P, TILES])
        r_u = sb("r_u", [P, TILES])
        mr_u = sb("mr_u", [P, TILES])
        mr_ua = sb("mr_ua", [P, TILES])
        c_u = sb("c_u", [P, TILES])
        w_out = sb("w_out", [P, TILES, D])
        o_sb = [sb(f"o_sb{i}", [P, TILES, D]) for i in range(2)]

        bank_s = [ctx.enter_context(nc.psum_tensor(f"bank_s{g}", [P, GT], F32)) for g in range(QUADS)]
        bank_a = ctx.enter_context(nc.psum_tensor("bank_a", [P, GT], F32))
        bank_b = ctx.enter_context(nc.psum_tensor("bank_b", [P, GT], F32))
        bank_c = ctx.enter_context(nc.psum_tensor("bank_c", [P, GT], F32))
        bank_o = ctx.enter_context(nc.psum_tensor("bank_o", [P, GT], F32))

        x_here = [sem(f"x_here{i}") for i in range(3)]
        w_here = sem("w_here")
        vecs_here = sem("vecs_here")
        cols_in_psum = sem("cols_in_psum")
        cols_ready = sem("cols_ready")
        rows_here = sem("rows_here")
        scales_here = sem("scales_here")
        quants_here = sem("quants_here")
        const_step = sem("const_step")
        ident_ready = sem("ident_ready")
        masks_ready = sem("masks_ready")
        jmask_ready = sem("jmask_ready")
        zeros_ready = sem("zeros_ready")
        bias_ready = sem("bias_ready")
        w_in_psum = sem("w_in_psum")
        w_ready = sem("w_ready")
        ffn_step = sem("ffn_step")
        ffn_ready = sem("ffn_ready")

        x_stats = sem("x_stats")
        x_mv = sem("x_mv")
        x_ve = sem("x_ve")
        x_rstd = sem("x_rstd")
        x_nm = sem("x_nm")
        x_norm_ready = sem("x_norm_ready")
        xn_ready = sem("xn_ready")
        xT_in_psum = sem("xT_in_psum")
        xT_ready = sem("xT_ready")
        k_in_psum = sem("k_in_psum")
        k_read = sem("k_read")
        q_in_psum = sem("q_in_psum")
        q_read = sem("q_read")
        v_in_psum = sem("v_in_psum")
        v_ready = sem("v_ready")
        kT_ready = sem("kT_ready")
        qT_ready = sem("qT_ready")
        kcum_ready = sem("kcum_ready")
        qkcum_ready = sem("qkcum_ready")
        ktok_in_psum = sem("ktok_in_psum")
        ktok_ready = sem("ktok_ready")
        state_in_psum = sem("state_in_psum")
        state_ready = sem("state_ready")
        den_in_psum = sem("den_in_psum")
        rden_ready = sem("rden_ready")
        rden_wide_ready = sem("rden_wide_ready")
        rdT_in_psum = sem("rdT_in_psum")
        qn_ready = sem("qn_ready")
        qm_ready = [sem(f"qm_ready{i}") for i in range(2)]
        scores_in_psum = [[sem(f"scores_in_psum{c}{g}") for g in range(QUADS)] for c in range(TILES)]
        scores_ready = [[sem(f"scores_ready{c}{g}") for g in range(QUADS)] for c in range(TILES)]
        o_in_psum = [sem(f"o_in_psum{c}") for c in range(TILES)]
        oT_ready = sem("oT_ready")
        wo_in_psum = sem("wo_in_psum")
        a_ready = sem("a_ready")
        a_stats = sem("a_stats")
        a_mv = sem("a_mv")
        a_ve = sem("a_ve")
        a_rstd = sem("a_rstd")
        a_mr = sem("a_mr")
        t_ready = sem("t_ready")
        t_stats = sem("t_stats")
        t_mv = sem("t_mv")
        t_ve = sem("t_ve")
        t_ve_res = sem("t_ve_res")
        t_rstd = sem("t_rstd")
        t_rstd_res = sem("t_rstd_res")
        t_nm = sem("t_nm")
        t_norm_ready = sem("t_norm_ready")
        z_ready = sem("z_ready")
        z_rest_ready = sem("z_rest_ready")
        hT_in_psum = sem("hT_in_psum")
        hT_ready = sem("hT_ready")
        fc1_in_psum = [sem(f"fc1_in_psum{i}") for i in range(FB)]
        act_ready = [sem(f"act_ready{i}") for i in range(FB)]
        fc2_in_psum = sem("fc2_in_psum")
        tr_ready = sem("tr_ready")
        res_ready = sem("res_ready")
        u_ready = sem("u_ready")
        u_stats = sem("u_stats")
        u_mv = sem("u_mv")
        u_ve = sem("u_ve")
        u_rstd = sem("u_rstd")
        u_mr = sem("u_mr")
        u_mra = sem("u_mra")
        u_c = sem("u_c")
        w_out_ready = sem("w_out_ready")
        o_ready = sem("o_ready")
        o_free = sem("o_free")
        stored = sem("stored")

        head_start = {e.name: 1 for e in (hT_in_psum, fc1_in_psum[FB - 1], fc2_in_psum, u_ready, u_c,
                                          w_out_ready, t_norm_ready, act_ready[2])}
        head_start[o_ready.name] = 2
        head_start[o_free.name] = 2

        class Group:

            def __init__(self, counts, off):
                self.counts, self.off = counts, off

            def __add__(self, n):
                return Group(self.counts, self.off + n)

            def __sub__(self, n):
                return Group(self.counts, self.off - n)

            def count(self):
                return self.counts[self.off]

        def after(eng, event, G):
            ahead = head_start.get(event.name, 0)
            if isinstance(G, int):
                if G >= 0:
                    eng.wait_ge(event, G + 1 + ahead)
            else:
                assert (G + 1 + ahead).off > -2, event.name
                eng.wait_ge(event, (G + 1 + ahead).count())

        def apart(eng):
            eng.wait_ge(ident_ready, 1)

        def steps(eng, step):
            step(0, 0)
            step(1, 1)
            with eng.Fori(1, NG // 2) as turn:
                counts = {off: eng.snap(turn * 2 + off) for off in range(-2, 4)}
                for count in counts.values():
                    eng.compute_val(count)
                step(Group(counts, 0), 0)
                step(Group(counts, 1), 1)
            step(NG, 0)
            step(NG + 1, 1)

        def comes_next(s):
            return not isinstance(s, int) or s + 1 < NG

        def x_tile(G, c):
            if isinstance(G, int):
                return x_all[:, G * GT + c * D:G * GT + (c + 1) * D]
            g = G.count() if G.off < 2 else G.count() & (NG - 1)
            return x_all[:, bass.ds(g * GT + c * D, D)]

        def has(s):
            if isinstance(s, int):
                return s < NG, 1 <= s <= NG, s >= 2
            return True, True, True

        block = ctx.enter_context(nc.Block())

        @block.sync
        def _(sp):
            def load_x(g0, g1, s_here):
                sp.dma_start(x_all[:, g0 * GT:g1 * GT].rearrange("p (t f) -> p t f", f=D),
                             x_d[:, g0 * TILES:g1 * TILES, :]).then_inc(s_here, 16)
            load_x(0, 1, x_here[0])
            for i, w in enumerate((Wq, Wk, Wv, Wo)):
                sp.dma_start(w_raw[:, i, :], w).then_inc(w_here, 16)
            load_x(1, 2, x_here[1])
            sp.dma_start(q1_sb[:], q1).then_inc(quants_here, 16)
            sp.dma_start(q2_sb[:], q2.rearrange("(k p) n -> p k n", p=P)).then_inc(quants_here, 16)
            load_x(2, NG, x_here[2])
            for e in (hT_in_psum, fc1_in_psum[FB - 1], fc2_in_psum, u_ready, u_c, w_out_ready,
                      t_norm_ready, act_ready[2], o_ready, o_free):
                sp.sem_inc(e, head_start[e.name])

            def store(s, p):
                if not has(s)[2]:
                    return
                G = s - 2
                after(sp, o_ready, G)
                if isinstance(G, int):
                    dst = out_d[:, G * TILES:(G + 1) * TILES, :]
                else:
                    dst = out_d[:, bass.ds(G.count() * TILES, TILES), :]
                sp.dma_start(dst, o_sb[p][:]).then_inc(stored, 16)
                sp.wait_ge(stored, 16 * (G + 1) if isinstance(G, int) else (G + 1).count() * 16)
                sp.sem_inc(o_free, 1)
            steps(sp, store)

        @block.gpsimd
        def _(pool):
            nc.gpsimd.memset(ident[:], 0.0).then_inc(const_step, 1)
            nc.gpsimd.memset(causal[:], 1.0).then_inc(const_step, 1)
            nc.gpsimd.memset(headsel[:], 1.0).then_inc(const_step, 1)
            nc.gpsimd.memset(expo[:], -0.5).then_inc(const_step, 1)
            nc.gpsimd.memset(ones[:], 1.0).then_inc(const_step, 1)
            pool.wait_ge(const_step, 5)
            nc.gpsimd.affine_select(out=ident[:], in_=ident[:], compare_op=ALU.not_equal, fill=1.0, base=0,
                                    pattern=[[-1, P]], channel_multiplier=1).then_inc(ident_ready, 1)
            nc.gpsimd.affine_select(out=causal[:], in_=causal[:], compare_op=ALU.is_ge, fill=0.0, base=0,
                                    pattern=[[1, P]], channel_multiplier=-1).then_inc(masks_ready, 1)
            nc.gpsimd.affine_select(out=headsel[:], in_=headsel[:], compare_op=ALU.is_ge, fill=0.0, base=0,
                                    pattern=[[-DH, H]], channel_multiplier=1).then_inc(const_step, 1)
            pool.wait_ge(const_step, 6)
            nc.gpsimd.affine_select(out=headsel[:], in_=headsel[:], compare_op=ALU.is_ge, fill=0.0, base=DH - 1,
                                    pattern=[[DH, H]], channel_multiplier=-1).then_inc(masks_ready, 1)

            def scale_x(G):
                apart(pool)
                after(pool, x_mv, G)
                after(pool, xn_ready, G - 1)
                nc.gpsimd.tensor_scalar(ve_x[:], mv_x[:, :, 1], 1.0, EPS, ALU.mult, ALU.add).then_inc(x_ve, 1)
                nc.gpsimd.tensor_scalar(nm_x[:], mv_x[:, :, 0], -1.0, 1.0, ALU.mult, ALU.mult).then_inc(x_nm, 1)
                after(pool, x_ve, G)
                nc.gpsimd.tensor_tensor(r_x[:], ve_x[:], expo[:, 0:TILES], ALU.pow).then_inc(x_rstd, 1)
                after(pool, x_rstd, G)
                after(pool, x_nm, G)
                nc.gpsimd.tensor_tensor(nb_x[:], nm_x[:], r_x[:], ALU.mult).then_inc(x_norm_ready, 1)

            def scale_t(G):
                apart(pool)
                after(pool, t_mv, G)
                nc.gpsimd.tensor_scalar(ve_t[:, 1, :], mv_t[:, :, 1], 1.0 + EPS, EPS * EPS, ALU.mult,
                                        ALU.add).then_inc(t_ve, 1)
                nc.gpsimd.tensor_scalar(nm_t[:], mv_t[:, :, 0], -1.0, 1.0, ALU.mult, ALU.mult).then_inc(t_nm, 1)
                nc.gpsimd.tensor_scalar(ve_t[:, 0, :], mv_t[:, :, 1], 1.0, EPS, ALU.mult, ALU.add).then_inc(t_ve_res, 1)
                after(pool, t_ve, G)
                nc.gpsimd.tensor_tensor(r_t[:, 1, :], ve_t[:, 1, :], expo[:, 0:TILES], ALU.pow).then_inc(t_rstd, 1)
                after(pool, t_rstd, G)
                after(pool, t_nm, G)
                nc.gpsimd.tensor_tensor(nb_t[:], nm_t[:], r_t[:, 1, :], ALU.mult).then_inc(t_norm_ready, 1)
                after(pool, t_ve_res, G)
                nc.gpsimd.tensor_tensor(r_t[:, 0, :], ve_t[:, 0, :], expo[:, 0:TILES], ALU.pow).then_inc(t_rstd_res, 1)

            scale_x(0)
            nc.gpsimd.memset(vpad[0][:], 0.0).then_inc(zeros_ready, 1)
            for v, dst in ((s1[0], s1_row[:]), (s2.rearrange("k n -> (k n)"), s2_row[:].rearrange("p k n -> p (k n)"))):
                pool.dma_start(dst, v.partition_broadcast(P)).then_inc(scales_here, 16)
            for v, dst in ((bo, bo_row), (b2, b2_row)):
                pool.dma_start(dst[:], v.partition_broadcast(P)).then_inc(rows_here, 16)
            nc.gpsimd.memset(vpad[1][:], 0.0).then_inc(zeros_ready, 1)

            def step(s, p):
                P_, S_, F_ = has(s)
                if F_ and s != NG + 1:
                    scale_t(s - 2)
                if P_:
                    G = s
                    after(pool, kcum_ready, G)
                    after(pool, qT_ready, G)
                    after(pool, den_in_psum, G - 1)
                    nc.gpsimd.tensor_tensor(qkcum[:], qT[:], kcum[:], ALU.mult).then_inc(qkcum_ready, 1)
                if comes_next(s):
                    scale_x(s + 1)
                if F_:
                    G, pf = s - 2, p
                    if isinstance(G, int) and G == 0:
                        pool.wait_ge(ffn_ready, 1)
                    apart(pool)
                    after(pool, u_ready, G - 1)
                    after(pool, t_ready, G)
                    after(pool, t_rstd_res, G)
                    for c in range(TILES):
                        i = nc.gpsimd.tensor_scalar(tr[:, c, :], t[pf][:, c, :], r_t[:, 0, c:c + 1], 1.0,
                                                    ALU.mult, ALU.mult)
                    i.then_inc(tr_ready, 1)
                    after(pool, tr_ready, G)
                    nc.gpsimd.tensor_tensor(res[:], tr[:], b2h_row[:, None, :].to_broadcast([P, TILES, D]),
                                            ALU.add).then_inc(res_ready, 1)
                if S_:
                    G, ps = s - 1, 1 - p
                    apart(pool)
                    after(pool, a_mv, G)
                    nc.gpsimd.tensor_scalar(ve_a[:], mv_a[:, :, 1], 1.0, EPS, ALU.mult, ALU.add).then_inc(a_ve, 1)
                    after(pool, a_ve, G)
                    nc.gpsimd.tensor_tensor(r_a[:], ve_a[:], expo[:, 0:TILES], ALU.pow).then_inc(a_rstd, 1)
                    after(pool, a_rstd, G)
                    nc.gpsimd.tensor_tensor(mr_a[ps][:], mv_a[:, :, 0], r_a[:], ALU.mult).then_inc(a_mr, 1)
                if s == NG:
                    scale_t(NG - 1)
                if F_:
                    G, pf = s - 2, p
                    apart(pool)
                    after(pool, u_mv, G)
                    nc.gpsimd.tensor_scalar(ve_u[:], mv_u[:, :, 1], 1.0, EPS, ALU.mult, ALU.add).then_inc(u_ve, 1)
                    after(pool, u_ve, G)
                    nc.gpsimd.tensor_tensor(r_u[:], ve_u[:], expo[:, 0:TILES], ALU.pow).then_inc(u_rstd, 1)
                    after(pool, u_rstd, G)
                    nc.gpsimd.tensor_tensor(mr_u[:], mv_u[:, :, 0], r_u[:], ALU.mult).then_inc(u_mr, 1)
                    after(pool, u_mr, G)
                    nc.gpsimd.tensor_tensor(mr_ua[:], mr_u[:], mr_a[pf][:], ALU.add).then_inc(u_mra, 1)
                    apart(pool)
                    after(pool, u_mra, G)
                    nc.gpsimd.tensor_scalar(c_u[:], mr_ua[:], -1.0, 1.0, ALU.mult, ALU.mult).then_inc(u_c, 1)
                if F_ and s != NG + 1:
                    G, pf = s - 2, p
                    apart(pool)
                    after(pool, u_c, G)
                    for c in range(TILES):
                        i = nc.gpsimd.tensor_scalar(w_out[:, c, :], u[:, c, :], r_u[:, c:c + 1], c_u[:, c:c + 1],
                                                    ALU.mult, ALU.add)
                    i.then_inc(w_out_ready, 1)
                    after(pool, w_out_ready, G)
                    after(pool, o_free, G - 2)
                    nc.gpsimd.tensor_tensor(o_sb[p][:], w_out[:], t[pf][:], ALU.add).then_inc(o_ready, 1)
            steps(pool, step)

        @block.scalar
        def _(act):
            for i, v in enumerate((bq, bk, bv, gamma, beta)):
                act.dma_start(vec_rows[i:i + 1, :], v[None, :]).then_inc(vecs_here, 16)
            act.dma_start(vec_rows[5:5 + FB, :], b1.rearrange("(k p) -> k p", p=P)).then_inc(vecs_here, 16)

            def normalise_x(G):
                after(act, x_norm_ready, G)
                after(act, xT_in_psum, G - 1)
                for c in range(TILES):
                    i = nc.scalar.activation(xn[:, c, :], x_tile(G, c), ACT.Identity, bias=nb_x[:, c:c + 1],
                                             scale=r_x[:, c:c + 1])
                i.then_inc(xn_ready, 1)

            def normalise_t(G, pf, tiles=TILES):
                after(act, t_norm_ready, G)
                after(act, t_ready, G)
                after(act, hT_in_psum, G - 1)
                for c in range(tiles):
                    i = nc.scalar.activation(z[:, c, :], t[pf][:, c, :], ACT.Identity, bias=nb_t[:, c:c + 1],
                                             scale=r_t[:, 1, c:c + 1])
                i.then_inc(z_ready, 1)

            def silu(s, i):
                G = s - 2
                if i == 0:
                    after(act, fc2_in_psum, G - 1)
                after(act, fc1_in_psum[i], G)
                nc.scalar.activation(act_h[:, i, :], (bank_a if i % 2 == 0 else bank_b)[:], ACT.Silu,
                                     bias=cols[:, 5 + i:6 + i]).then_inc(act_ready[i], 1)

            normalise_x(0)
            act.wait_ge(w_in_psum, 1)
            nc.scalar.activation(wT[:].rearrange("p k n -> p (k n)"), bank_o[:], ACT.Copy).then_inc(w_ready, 1)
            act.wait_ge(cols_in_psum, 1)
            nc.scalar.activation(cols[:], bank_b[:, 0:5 + FB], ACT.Copy).then_inc(cols_ready, 1)
            act.wait_ge(cols_ready, 1)

            def step(s, p):
                P_, S_, F_ = has(s)
                if P_:
                    G = s
                    after(act, xT_in_psum, G)
                    after(act, v_in_psum, G - 1)
                    nc.scalar.activation(xnT[:], bank_a[:], ACT.Copy).then_inc(xT_ready, 1)
                    after(act, k_in_psum, G)
                    after(act, kT_ready, G - 1)
                    nc.scalar.activation(k_exp[:], bank_a[:], ACT.Exp, bias=cols[:, 1:2])
                    if isinstance(G, int) and G == 0:
                        act.wait_ge(bias_ready, 1)
                    nc.scalar.activation(k_lin[:], bank_a[:], ACT.Identity, bias=bq1[:, 1:2]).then_inc(k_read, 1)
                if P_:
                    G = s
                    after(act, q_in_psum, G)
                    after(act, qT_ready, G - 1)
                    nc.scalar.activation(q_exp[:], bank_b[:], ACT.Exp, bias=cols[:, 0:1])
                    nc.scalar.activation(q_lin[:], bank_b[:], ACT.Identity, bias=bq1[:, 0:1]).then_inc(q_read, 1)
                if F_ and s != NG + 1:
                    normalise_t(s - 2, p)
                if P_:
                    G = s
                    after(act, v_in_psum, G)
                    if isinstance(G, int) and G < 2:
                        act.wait_ge(zeros_ready, G + 1)
                    after(act, o_in_psum[TILES - 1], G - 2)
                    for c in range(TILES):
                        dst = vpad[p][:, c, :].rearrange("p (j r) -> p j r", j=JH)[:, :, 0:P]
                        dst = dst.rearrange("p j (g r) -> p j g r", g=QUADS)[:, :, :, 0:DH]
                        dst = dst.rearrange("p j g e -> p g j e")
                        src = bank_b[:, c * P:(c + 1) * P].rearrange("p (g j e) -> p g j e", g=QUADS, j=JH)
                        i = nc.scalar.activation(dst, src, ACT.Copy)
                    i.then_inc(v_ready, 1)
                if F_:
                    G = s - 2
                    after(act, hT_in_psum, G)
                    after(act, fc1_in_psum[FB - 1], G - 1)
                    nc.scalar.activation(hT[:], bank_c[:], ACT.Identity, bias=cols[:, 4:5],
                                         scale=cols[:, 3:4]).then_inc(hT_ready, 1)
                first = isinstance(s, int) and s == 0
                if comes_next(s) and not first:
                    normalise_x(s + 1)
                if F_:
                    nc.scalar.activation(scrap[:], expo[:, 0:1], ACT.Silu)
                if P_:
                    G = s
                    after(act, rden_ready, G)
                    after(act, rdT_in_psum, G - 1)
                    nc.scalar.activation(rden_wide[:].rearrange("p t (h e) -> p (t h) e", e=DH),
                                         rden[:, :, None].to_broadcast([P, TILES * H, DH]),
                                         ACT.Copy).then_inc(rden_wide_ready, 1)
                if F_:
                    silu(s, 0)
                    silu(s, 1)
                if S_:
                    G = s - 1
                    after(act, o_in_psum[TILES - 1], G)
                    after(act, wo_in_psum, G - 1)
                    nc.scalar.activation(oT[:], bank_o[:], ACT.Identity, bias=cols[:, 2:3]).then_inc(oT_ready, 1)
                if P_:
                    G = s
                    after(act, ktok_in_psum, G)
                    after(act, state_in_psum, G - 1)
                    nc.scalar.activation(ktok[:].rearrange("p b f -> p (b f)"), bank_c[:, 0:2 * D],
                                         ACT.Copy).then_inc(ktok_ready, 1)
                    if isinstance(G, int) and G == 0:
                        act.wait_ge(jmask_ready, 1)
                    after(act, qn_ready, G)
                    after(act, scores_in_psum[TILES - 1][QUADS - 1], G - 2)
                    for j in range(QM_ACT):
                        i = nc.scalar.activation(qm[p][:, :, j, :], qn[p][:].rearrange("p (t q) -> p t q", q=P),
                                                 ACT.Copy, scale=jmask[:, j:j + 1])
                    i.then_inc(qm_ready[0], 1)
                if first:
                    normalise_x(s + 1)
                if F_:
                    silu(s, 2)
                    silu(s, 3)
                if s == NG:
                    normalise_t(NG - 1, 1, TILES // 2)
            steps(act, step)

        @block.vector
        def _(dve):
            def moments(src, stat, mv, s_stat, s_mv, G):
                for c in range(TILES):
                    i = nc.vector.bn_stats(stat[:, c, :], src(c))
                i.then_inc(s_stat, 1)
                apart(dve)
                after(dve, s_stat, G)
                for c in range(TILES):
                    i = nc.vector.bn_aggr(mv[:, c, :], stat[:, c, :])
                i.then_inc(s_mv, 1)

            def mask_scores(G, first, end):
                for c, g in PARTS[first:end]:
                    after(dve, scores_in_psum[c][g], G)
                    if g == 0:
                        if c < 2:
                            after(dve, o_in_psum[c + 2], G - 1)
                        else:
                            after(dve, o_in_psum[c - 2], G)
                    nc.vector.tensor_tensor(sm[c % 2][:, g, :].rearrange("p (j q) -> p j q", j=JH),
                                            bank_s[g][:].rearrange("p (j q) -> p j q", j=JH),
                                            causal[:, None, :].to_broadcast([P, JH, P]),
                                            ALU.mult).then_inc(scores_ready[c][g], 1)

            def setup_ffn():
                dve.wait_ge(quants_here, 32)
                dve.wait_ge(scales_here, 32)
                nc.vector.tensor_scalar(w1[:], q1_sb[:], -128.0, None, ALU.add).then_inc(ffn_step, 1)
                nc.vector.tensor_scalar(w2h[:], q2_sb[:], -128.0, 0.5, ALU.add, ALU.mult).then_inc(ffn_step, 1)
                dve.wait_ge(ffn_step, 2)
                nc.vector.tensor_tensor(w1[:], w1[:], s1_row[:], ALU.mult)
                nc.vector.tensor_tensor(w2h[:], w2h[:], s2_row[:], ALU.mult)
                dve.wait_ge(rows_here, 32)
                nc.vector.tensor_scalar(b2h_row[:], b2_row[:], 0.5, None, ALU.mult).then_inc(ffn_ready, 1)

            def stats_x(G):
                if isinstance(G, int) and G < 3:
                    dve.wait_ge(x_here[G], 16)
                after(dve, x_norm_ready, G - 1)
                moments(lambda c: x_tile(G, c), stat_x, mv_x, x_stats, x_mv, G)

            def last_output(G, pf):
                after(dve, u_rstd, G)
                after(dve, u_c, G)
                for c in range(TILES):
                    i = nc.vector.tensor_scalar(w_out[:, c, :], u[:, c, :], r_u[:, c:c + 1], c_u[:, c:c + 1],
                                                ALU.mult, ALU.add)
                i.then_inc(w_out_ready, 1)
                after(dve, w_out_ready, G)
                after(dve, o_free, G - 2)
                nc.vector.tensor_tensor(o_sb[pf][:], w_out[:], t[pf][:], ALU.add).then_inc(o_ready, 1)

            def first_residual(G, pf):
                after(dve, a_rstd, G)
                after(dve, o_ready, G - 2)
                for c in range(TILES):
                    i = nc.vector.scalar_tensor_tensor(t[pf][:, c, :], a_sb[:, c, :], r_a[:, c:c + 1],
                                                       x_tile(G, c), ALU.mult, ALU.add)
                i.then_inc(t_ready, 1)
                after(dve, t_ready, G)
                after(dve, t_norm_ready, G - 1)
                moments(lambda c: t[pf][:, c, :], stat_t, mv_t, t_stats, t_mv, G)

            stats_x(0)

            def step(s, p):
                P_, S_, F_ = has(s)
                first = isinstance(s, int) and s == 0
                if first:
                    dve.wait_ge(cols_ready, 1)
                    nc.vector.tensor_scalar(bq1[:], cols[:, 0:2], 1.0, None, ALU.add).then_inc(bias_ready, 1)
                    dve.wait_ge(masks_ready, 2)
                    nc.vector.tensor_copy(blockdiag[:].rearrange("p (h e) -> p h e", e=DH),
                                          headsel[:, :, None].to_broadcast([P, H, DH]))
                    nc.vector.tensor_reduce(jmask[:], headsel[:].rearrange("p (g j) -> p j g", g=QUADS), AX_X,
                                            ALU.add).then_inc(jmask_ready, 1)
                if S_:
                    mask_scores(s - 1, 6, 8)
                if F_ and s != NG + 1:
                    first_residual(s - 2, p)
                if S_:
                    mask_scores(s - 1, 8, 10)
                if P_:
                    G = s
                    after(dve, k_read, G)
                    after(dve, scores_in_psum[TILES - 1][QUADS - 1], G - 2)
                    nc.vector.scalar_tensor_tensor(kT[p][:], k_exp[:], 1.0, k_lin[:], ALU.min, ALU.max).then_inc(kT_ready, 1)
                if S_:
                    mask_scores(s - 1, 10, 12)
                if P_:
                    G = s
                    after(dve, kT_ready, G)
                    after(dve, qkcum_ready, G - 1)
                    for b in range(2):
                        cut = slice(b * 2 * P, (b + 1) * 2 * P)
                        i = nc.vector.tensor_tensor_scan(kcum[:, cut], ones[:], kT[p][:, cut], 0.0, ALU.mult, ALU.add)
                    i.then_inc(kcum_ready, 1)
                    after(dve, q_read, G)
                    nc.vector.scalar_tensor_tensor(qT[:], q_exp[:], 1.0, q_lin[:], ALU.min, ALU.max).then_inc(qT_ready, 1)
                if S_:
                    mask_scores(s - 1, 12, 14)
                if comes_next(s):
                    stats_x(s + 1)
                if S_:
                    mask_scores(s - 1, 14, 16)
                if P_:
                    G = s
                    after(dve, den_in_psum, G)
                    after(dve, rden_wide_ready, G - 1)
                    nc.vector.reciprocal(rden[:], bank_c[:, 0:TILES * H]).then_inc(rden_ready, 1)
                    after(dve, rdT_in_psum, G)
                    after(dve, o_in_psum[TILES - 1], G - 2)
                    nc.vector.tensor_tensor(qn[p][:], bank_c[:], qT[:], ALU.mult).then_inc(qn_ready, 1)
                    if first:
                        dve.wait_ge(jmask_ready, 1)
                    after(dve, qn_ready, G)
                    for j in range(QM_ACT, JH):
                        i = nc.vector.tensor_scalar(qm[p][:, :, j, :], qn[p][:].rearrange("p (t q) -> p t q", q=P),
                                                    jmask[:, j:j + 1], None, ALU.mult)
                    i.then_inc(qm_ready[1], 1)
                    after(dve, state_in_psum, G)
                    nc.vector.tensor_tensor(state[p][:], bank_c[:, 0:2 * D].rearrange("p (b f) -> p b f", b=2),
                                            blockdiag[:, None, :].to_broadcast([P, 2, D]), ALU.mult).then_inc(state_ready, 1)
                if P_:
                    mask_scores(s, 0, 3)
                if S_:
                    G = s - 1
                    after(dve, wo_in_psum, G)
                    after(dve, t_ready, G - 1)
                    nc.vector.tensor_tensor(a_sb[:], bank_c[:].rearrange("p (t f) -> p t f", f=D),
                                            bo_row[:, None, :].to_broadcast([P, TILES, D]), ALU.add).then_inc(a_ready, 1)
                    after(dve, a_ready, G)
                    after(dve, a_mr, G - 1)
                    moments(lambda c: a_sb[:, c, :], stat_a, mv_a, a_stats, a_mv, G)
                if s == NG:
                    first_residual(NG - 1, 1)
                if P_:
                    mask_scores(s, 3, 6)
                if first:
                    setup_ffn()
                if F_:
                    G = s - 2
                    after(dve, fc2_in_psum, G)
                    after(dve, res_ready, G)
                    after(dve, w_out_ready, G - 1)
                    nc.vector.tensor_tensor(u[:].rearrange("p t f -> p (t f)"), bank_b[:],
                                            res[:].rearrange("p t f -> p (t f)"), ALU.add).then_inc(u_ready, 1)
                    after(dve, u_ready, G)
                    after(dve, u_c, G - 1)
                    moments(lambda c: u[:, c, :], stat_u, mv_u, u_stats, u_mv, G)
                if s == NG:
                    after(dve, t_norm_ready, NG - 1)
                    after(dve, hT_in_psum, NG - 2)
                    for c in range(TILES // 2, TILES):
                        i = nc.vector.tensor_scalar(z[:, c, :], t[1][:, c, :], r_t[:, 1, c:c + 1], nb_t[:, c:c + 1],
                                                    ALU.mult, ALU.add)
                    i.then_inc(z_rest_ready, 1)
                if s == NG + 1:
                    last_output(NG - 1, 1)
            steps(dve, step)

        @block.tensor
        def _(pe):
            def warm_up(n):
                for _ in range(n):
                    nc.tensor.matmul(bank_a[:, 0:2 * P], ident[:], ones[:], start=True, stop=True)

            pe.wait_ge(ident_ready, 1)
            warm_up(6)
            pe.wait_ge(w_here, 64)
            for i in range(4):
                last = nc.tensor.transpose(bank_o[:, i * P:(i + 1) * P], w_raw[:, i, :], ident[:])
            last.then_inc(w_in_psum, 1)
            pe.wait_ge(vecs_here, 96)
            nc.tensor.transpose(bank_b[:, 0:5 + FB], vec_rows[:], ident[0:5 + FB, 0:5 + FB]).then_inc(cols_in_psum, 1)
            warm_up(3)
            WQ, WK, WV, WO = (wT[:, i, :] for i in range(4))

            def tile(c):
                return slice(c * P, (c + 1) * P)

            def scores(G, ps, first, end):
                for c, g in PARTS[first:end]:
                    if c == 0:
                        if g == 0:
                            after(pe, qm_ready[0], G)
                            after(pe, qm_ready[1], G)
                        after(pe, scores_ready[TILES - 1][g], G - 1)
                    else:
                        after(pe, scores_ready[c - 1][g], G)
                    rows = slice(32 * g, 32 * g + 32)
                    nc.tensor.matmul(bank_s[g][:], kT[ps][rows, tile(c)],
                                     qm[ps][rows, c, :, :].rearrange("p j q -> p (j q)"),
                                     start=True, stop=True).then_inc(scores_in_psum[c][g], 1)

            def numerators(s, p, c):
                G, ps = s - 1, 1 - p
                if c == 0:
                    after(pe, oT_ready, G - 1)
                after_state = c % 2 == 1
                if after_state:
                    nc.tensor.matmul(bank_o[:, tile(c)], state[ps][:, c // 2, :], qn[ps][:, tile(c)],
                                     start=True, stop=False, skip_group_check=True)
                for g in range(QUADS):
                    after(pe, scores_ready[c][g], G)
                for j in range(JH):
                    for g in range(QUADS):
                        last = nc.tensor.matmul(bank_o[32 * g:32 * g + 32, tile(c)],
                                                vpad[ps][:, c, j * P + 32 * g:j * P + 32 * g + 32],
                                                sm[c % 2][:, g, tile(j)],
                                                start=j == 0 and not after_state, stop=j == JH - 1,
                                                skip_group_check=True)
                last.then_inc(o_in_psum[c], 1)

            def fc1(s, i):
                G = s - 2
                nc.tensor.matmul((bank_a if i % 2 == 0 else bank_b)[:], w1[:, tile(i)], hT[:],
                                 start=True, stop=True).then_inc(fc1_in_psum[i], 1)

            def output_projection(s, P_):
                G = s - 1
                after(pe, oT_ready, G)
                if P_:
                    after(pe, state_ready, s)
                else:
                    after(pe, hT_ready, s - 2)
                for c in range(TILES):
                    last = nc.tensor.matmul(bank_c[:, tile(c)], oT[:, tile(c)], WO, start=True, stop=True)
                last.then_inc(wo_in_psum, 1)

            def keep_warm(bank):
                nc.tensor.matmul(bank[:], ident[:], wT[:].rearrange("p k n -> p (k n)"), start=True, stop=True)

            def v_tiles(first, end):
                for c in range(first, end):
                    last = nc.tensor.matmul(bank_b[:, tile(c)], xnT[:, tile(c)], WV, start=True, stop=True)
                return last

            def fc2(s, first, end):
                for c in range(first, end):
                    for i in range(FB):
                        last = nc.tensor.matmul(bank_b[:, tile(c)], act_h[:, i, tile(c)], w2h[:, i, :],
                                                start=i == 0, stop=i == FB - 1)
                return last

            def step(s, p):
                P_, S_, F_ = has(s)
                if P_:
                    G = s
                    after(pe, xn_ready, G)
                    after(pe, k_read, G - 1)
                    after(pe, act_ready[2], G - 3)
                    for c in range(TILES):
                        last = nc.tensor.transpose(bank_a[:, tile(c)], xn[:, c, :], ident[:])
                    last.then_inc(xT_in_psum, 1)
                if S_:
                    scores(s - 1, 1 - p, 6, 8)
                    numerators(s, p, 0)
                if P_:
                    G = s
                    if isinstance(G, int) and G == 0:
                        pe.wait_ge(w_ready, 1)
                    after(pe, xT_ready, G)
                    nc.tensor.matmul(bank_a[:], WK, xnT[:], start=True, stop=True).then_inc(k_in_psum, 1)
                if S_:
                    scores(s - 1, 1 - p, 8, 11)
                if P_:
                    G = s
                    after(pe, u_ready, G - 3)
                    if isinstance(G, int) and G == 0:
                        pe.wait_ge(cols_ready, 1)
                    nc.tensor.matmul(bank_b[:], WQ, xnT[:], start=True, stop=True).then_inc(q_in_psum, 1)
                elif S_:
                    after(pe, act_ready[2], s - 3)
                    keep_warm(bank_a)
                if S_:
                    scores(s - 1, 1 - p, 11, 12)
                    numerators(s, p, 1)
                if P_:
                    G = s
                    after(pe, q_read, G)
                    v_tiles(0, 2)
                elif S_:
                    keep_warm(bank_a)
                if S_:
                    scores(s - 1, 1 - p, 12, 14)
                if P_:
                    v_tiles(2, 4).then_inc(v_in_psum, 1)
                if F_:
                    G = s - 2
                    if s == NG + 1:
                        for _ in range(6):
                            keep_warm(bank_a)
                        pe.wait_ge(z_rest_ready, 1)
                    after(pe, z_ready, G)
                    after(pe, a_ready, G)
                    for c in range(TILES):
                        last = nc.tensor.transpose(bank_c[:, tile(c)], z[:, c, :], ident[:])
                    last.then_inc(hT_in_psum, 1)
                if S_:
                    scores(s - 1, 1 - p, 14, 16)
                if F_:
                    G = s - 2
                    if P_:
                        after(pe, k_read, s)
                    else:
                        after(pe, act_ready[2], G - 1)
                    if isinstance(G, int) and G == 0:
                        pe.wait_ge(ffn_ready, 1)
                    after(pe, hT_ready, G)
                    fc1(s, 0)
                else:
                    after(pe, k_read, s)
                    keep_warm(bank_a)
                if S_:
                    numerators(s, p, 2)
                if P_:
                    G = s
                    after(pe, qkcum_ready, G)
                    after(pe, hT_ready, G - 2)
                    if isinstance(G, int) and G == 1:
                        after(pe, state_ready, 0)
                    for c in range(TILES):
                        last = nc.tensor.matmul(bank_c[:, c * H:(c + 1) * H], qkcum[:, tile(c)], headsel[:],
                                                start=True, stop=True)
                    last.then_inc(den_in_psum, 1)
                if F_:
                    if P_:
                        after(pe, v_ready, s)
                    else:
                        after(pe, u_ready, s - 3)
                    fc1(s, 1)
                if S_:
                    numerators(s, p, 3)
                if P_:
                    G = s
                    after(pe, rden_wide_ready, G)
                    for c in range(TILES):
                        last = nc.tensor.matmul(bank_c[:, tile(c)], rden_wide[:, c, :],
                                                ident[:], start=True, stop=True, is_transpose=True)
                    last.then_inc(rdT_in_psum, 1)
                if F_:
                    after(pe, act_ready[0], s - 2)
                    fc1(s, 2)
                else:
                    keep_warm(bank_a)
                if P_:
                    G = s
                    after(pe, kT_ready, G)
                    after(pe, qn_ready, G)
                    for b in range(2):
                        last = nc.tensor.transpose(bank_c[:, tile(b)], kT[p][:, tile(2 * b)], ident[:])
                    last.then_inc(ktok_in_psum, 1)
                if S_ and not P_:
                    output_projection(s, P_)
                if F_:
                    after(pe, act_ready[1], s - 2)
                    fc1(s, 3)
                else:
                    keep_warm(bank_a)
                if P_:
                    G = s
                    after(pe, ktok_ready, G)
                    after(pe, v_ready, G)
                    for b in range(2):
                        v_rows = vpad[p][:, 2 * b, :].rearrange("p (j r) -> p j r", j=JH)[:, :, 0:P]
                        v_rows = v_rows.rearrange("p j (g r) -> p j g r", g=QUADS)[:, :, :, 0:DH]
                        last = nc.tensor.matmul(bank_c[:, tile(b)], ktok[:, b, :],
                                                v_rows.rearrange("p j g e -> p g j e"), start=True, stop=True)
                    last.then_inc(state_in_psum, 1)
                if P_:
                    scores(s, p, 0, 3)
                if S_ and P_:
                    output_projection(s, P_)
                if F_:
                    after(pe, act_ready[FB - 1], s - 2)
                    fc2(s, 0, 2)
                else:
                    keep_warm(bank_a)
                if P_:
                    scores(s, p, 3, 6)
                if F_:
                    fc2(s, 2, 4).then_inc(fc2_in_psum, 1)
                else:
                    keep_warm(bank_a)
            steps(pe, step)


_INS = ['L0_attn_x', 'L0_attn_Wq', 'L0_attn_bq', 'L0_attn_Wk', 'L0_attn_bk', 'L0_attn_Wv', 'L0_attn_bv',
        'L0_attn_Wo', 'L0_attn_bo', 'L0_ffn_ln_gamma', 'L0_ffn_ln_beta', 'L0_ffn_fc1_q', 'L0_ffn_fc1_scales',
        'L0_ffn_fc1_bias', 'L0_ffn_fc2_q', 'L0_ffn_fc2_scales', 'L0_ffn_fc2_bias']


def kernel(**inputs):
    import concourse.bacc as bacc
    from concourse.bass_utils import run_bass_kernel_spmd

    nc = bacc.Bacc("TRN2", target_bir_lowering=False, num_devices=1)
    arrays, args = {}, []
    for name in _INS:
        a = np.ascontiguousarray(inputs[name])
        arrays[name] = a
        args.append(nc.dram_tensor(name, a.shape, mybir.dt.from_np(a.dtype), kind="ExternalInput").ap())
    shape = arrays['L0_attn_x'].shape
    args.append(nc.dram_tensor("y", shape, F32, kind="ExternalOutput").ap())
    build(nc, *args)
    return run_bass_kernel_spmd(nc, [arrays], core_ids=[0]).results[0]["y"]
```
